# Optimizing a Trainium2 kernel written in Bass

```python
import numpy as np
import jax
import jax.numpy as jnp

def _softmax(x, axis=-1):
    return jax.nn.softmax(x, axis=axis)

def _gelu(x):
    return jax.nn.gelu(x, approximate=True)

def _silu(x):
    return jax.nn.silu(x)

def _sigmoid(x):
    return jax.nn.sigmoid(x)

def _layernorm(x, axis=-1, eps=1e-05):
    m = jnp.mean(x, axis=axis, keepdims=True)
    v = jnp.var(x, axis=axis, keepdims=True)
    return (x - m) / jnp.sqrt(v + eps)

def _scatter_add(tgt, idx, src, axis=0):
    return tgt.at[idx].add(src)

def _segment_sum(src, seg, n):
    return jax.ops.segment_sum(src, seg, n)
kernel_name = 'mk_dlrm_tower_d1_rec_r8_0f5ca0'

def setup_inputs(seed: int=0):
    np.random.seed(seed)
    _w = jnp.asarray

    def _rec_inputs():
        import jax
        import jax.numpy as jnp
        _tk = jax.random.key(seed)
        ids = jnp.stack([jax.random.randint(jax.random.fold_in(_tk, 200 + f), (512,), 0, v, jnp.int32) for f, v in enumerate([125000, 12500, 1000, 1250, 12500, 1000, 1000, 12500, 1250, 1000, 1250, 1000, 1000, 1000, 1250, 12500, 12500, 1000, 1250, 1250, 12500, 12500, 1000, 1000, 12500, 1000])], axis=1)
        tbl_0 = 0.05 * jax.random.normal(jax.random.fold_in(_tk, 500 + 0), (125000, 128), jnp.float32)
        tbl_1 = 0.05 * jax.random.normal(jax.random.fold_in(_tk, 500 + 1), (12500, 128), jnp.float32)
        tbl_2 = 0.05 * jax.random.normal(jax.random.fold_in(_tk, 500 + 2), (1000, 128), jnp.float32)
        tbl_3 = 0.05 * jax.random.normal(jax.random.fold_in(_tk, 500 + 3), (1250, 128), jnp.float32)
        tbl_4 = 0.05 * jax.random.normal(jax.random.fold_in(_tk, 500 + 4), (12500, 128), jnp.float32)
        tbl_5 = 0.05 * jax.random.normal(jax.random.fold_in(_tk, 500 + 5), (1000, 128), jnp.float32)
        tbl_6 = 0.05 * jax.random.normal(jax.random.fold_in(_tk, 500 + 6), (1000, 128), jnp.float32)
        tbl_7 = 0.05 * jax.random.normal(jax.random.fold_in(_tk, 500 + 7), (12500, 128), jnp.float32)
        tbl_8 = 0.05 * jax.random.normal(jax.random.fold_in(_tk, 500 + 8), (1250, 128), jnp.float32)
        tbl_9 = 0.05 * jax.random.normal(jax.random.fold_in(_tk, 500 + 9), (1000, 128), jnp.float32)
        tbl_10 = 0.05 * jax.random.normal(jax.random.fold_in(_tk, 500 + 10), (1250, 128), jnp.float32)
        tbl_11 = 0.05 * jax.random.normal(jax.random.fold_in(_tk, 500 + 11), (1000, 128), jnp.float32)
        tbl_12 = 0.05 * jax.random.normal(jax.random.fold_in(_tk, 500 + 12), (1000, 128), jnp.float32)
        tbl_13 = 0.05 * jax.random.normal(jax.random.fold_in(_tk, 500 + 13), (1000, 128), jnp.float32)
        tbl_14 = 0.05 * jax.random.normal(jax.random.fold_in(_tk, 500 + 14), (1250, 128), jnp.float32)
        tbl_15 = 0.05 * jax.random.normal(jax.random.fold_in(_tk, 500 + 15), (12500, 128), jnp.float32)
        tbl_16 = 0.05 * jax.random.normal(jax.random.fold_in(_tk, 500 + 16), (12500, 128), jnp.float32)
        tbl_17 = 0.05 * jax.random.normal(jax.random.fold_in(_tk, 500 + 17), (1000, 128), jnp.float32)
        tbl_18 = 0.05 * jax.random.normal(jax.random.fold_in(_tk, 500 + 18), (1250, 128), jnp.float32)
        tbl_19 = 0.05 * jax.random.normal(jax.random.fold_in(_tk, 500 + 19), (1250, 128), jnp.float32)
        tbl_20 = 0.05 * jax.random.normal(jax.random.fold_in(_tk, 500 + 20), (12500, 128), jnp.float32)
        tbl_21 = 0.05 * jax.random.normal(jax.random.fold_in(_tk, 500 + 21), (12500, 128), jnp.float32)
        tbl_22 = 0.05 * jax.random.normal(jax.random.fold_in(_tk, 500 + 22), (1000, 128), jnp.float32)
        tbl_23 = 0.05 * jax.random.normal(jax.random.fold_in(_tk, 500 + 23), (1000, 128), jnp.float32)
        tbl_24 = 0.05 * jax.random.normal(jax.random.fold_in(_tk, 500 + 24), (12500, 128), jnp.float32)
        tbl_25 = 0.05 * jax.random.normal(jax.random.fold_in(_tk, 500 + 25), (1000, 128), jnp.float32)
        _rk = jax.random.fold_in(_tk, 7)
        r_dense_features = -0.000520686 + 1.00062 * jax.random.normal(jax.random.fold_in(_rk, 101), (512, 128), jnp.float32)
        W_top1 = 0.0405887 * jax.random.normal(jax.random.fold_in(_tk, 801), (607, 512), jnp.float32)
        W_top2 = 0.0441942 * jax.random.normal(jax.random.fold_in(_tk, 802), (512, 256), jnp.float32)
        W_top3 = 0.0625 * jax.random.normal(jax.random.fold_in(_tk, 803), (256, 1), jnp.float32)
        b_top1 = jnp.zeros((512,), jnp.float32)
        b_top2 = jnp.zeros((256,), jnp.float32)
        return (r_dense_features, ids, tbl_0, tbl_1, tbl_2, tbl_3, tbl_4, tbl_5, tbl_6, tbl_7, tbl_8, tbl_9, tbl_10, tbl_11, tbl_12, tbl_13, tbl_14, tbl_15, tbl_16, tbl_17, tbl_18, tbl_19, tbl_20, tbl_21, tbl_22, tbl_23, tbl_24, tbl_25, W_top1, b_top1, W_top2, b_top2, W_top3)
    r_dense_features, ids, tbl_0, tbl_1, tbl_2, tbl_3, tbl_4, tbl_5, tbl_6, tbl_7, tbl_8, tbl_9, tbl_10, tbl_11, tbl_12, tbl_13, tbl_14, tbl_15, tbl_16, tbl_17, tbl_18, tbl_19, tbl_20, tbl_21, tbl_22, tbl_23, tbl_24, tbl_25, W_top1, b_top1, W_top2, b_top2, W_top3 = _rec_inputs()

    def _L0_rec_setup():
        import jax, jax.numpy as jnp
        import numpy as np
        B, F, D = (2048, 26, 128)
        key = jax.random.key(seed)
        k1, k2 = jax.random.split(key)
        dense_features = jax.random.normal(k1, (B, D), dtype=jnp.float32)
        sparse_values = jax.random.normal(k2, (B, F, D), dtype=jnp.float32)
        return {'dense_features': dense_features, 'sparse_values': sparse_values}
    _L0_rec_all = _L0_rec_setup()
    _L0_rec_in = {k: v for k, v in _L0_rec_all.items() if k in ()}
    del _L0_rec_all
    return {'r_dense_features': r_dense_features, 'ids': ids, 'tbl_0': tbl_0, 'tbl_1': tbl_1, 'tbl_2': tbl_2, 'tbl_3': tbl_3, 'tbl_4': tbl_4, 'tbl_5': tbl_5, 'tbl_6': tbl_6, 'tbl_7': tbl_7, 'tbl_8': tbl_8, 'tbl_9': tbl_9, 'tbl_10': tbl_10, 'tbl_11': tbl_11, 'tbl_12': tbl_12, 'tbl_13': tbl_13, 'tbl_14': tbl_14, 'tbl_15': tbl_15, 'tbl_16': tbl_16, 'tbl_17': tbl_17, 'tbl_18': tbl_18, 'tbl_19': tbl_19, 'tbl_20': tbl_20, 'tbl_21': tbl_21, 'tbl_22': tbl_22, 'tbl_23': tbl_23, 'tbl_24': tbl_24, 'tbl_25': tbl_25, 'W_top1': W_top1, 'b_top1': b_top1, 'W_top2': W_top2, 'b_top2': b_top2, 'W_top3': W_top3}

def reference(r_dense_features, ids, tbl_0, tbl_1, tbl_2, tbl_3, tbl_4, tbl_5, tbl_6, tbl_7, tbl_8, tbl_9, tbl_10, tbl_11, tbl_12, tbl_13, tbl_14, tbl_15, tbl_16, tbl_17, tbl_18, tbl_19, tbl_20, tbl_21, tbl_22, tbl_23, tbl_24, tbl_25, W_top1, b_top1, W_top2, b_top2, W_top3):
    import jax
    import jax.numpy as jnp

    def _L0_rec_ref(dense_features, sparse_values):
        import jax, jax.numpy as jnp
        import numpy as np
        B, F, D = (2048, 26, 128)
        sd = jnp.einsum('bfd,bd->bf', sparse_values, dense_features)
        ss = jnp.einsum('bfd,bgd->bfg', sparse_values, sparse_values)
        iu, ju = jnp.triu_indices(F, k=1)
        pairs = ss[:, iu, ju]
        return jnp.concatenate([dense_features, sd, pairs], axis=1)
    e = jnp.stack([tbl_0[ids[:, 0]], tbl_1[ids[:, 1]], tbl_2[ids[:, 2]], tbl_3[ids[:, 3]], tbl_4[ids[:, 4]], tbl_5[ids[:, 5]], tbl_6[ids[:, 6]], tbl_7[ids[:, 7]], tbl_8[ids[:, 8]], tbl_9[ids[:, 9]], tbl_10[ids[:, 10]], tbl_11[ids[:, 11]], tbl_12[ids[:, 12]], tbl_13[ids[:, 13]], tbl_14[ids[:, 14]], tbl_15[ids[:, 15]], tbl_16[ids[:, 16]], tbl_17[ids[:, 17]], tbl_18[ids[:, 18]], tbl_19[ids[:, 19]], tbl_20[ids[:, 20]], tbl_21[ids[:, 21]], tbl_22[ids[:, 22]], tbl_23[ids[:, 23]], tbl_24[ids[:, 24]], tbl_25[ids[:, 25]]], axis=1)
    z = _L0_rec_ref(r_dense_features, e)
    z = z.reshape(z.shape[0], -1)
    h = jnp.concatenate([z, r_dense_features], axis=1)
    h = jnp.maximum(h @ W_top1 + b_top1, 0.0)
    h = jnp.maximum(h @ W_top2 + b_top2, 0.0)
    y = h @ W_top3
    return y

_drawn_inputs = setup_inputs


def setup_inputs(seed=0):
    import zlib

    import numpy as np

    out = dict(_drawn_inputs(seed))
    spreads = {'b_top1': (0.0, 0.1), 'b_top2': (0.0, 0.1)}
    factors = {}
    for name, (base, spread) in spreads.items():
        noise = np.random.default_rng([zlib.crc32(name.encode()), seed]).standard_normal(out[name].shape)
        drawn = base * np.exp(spread * noise) if base else spread * noise
        out[name] = jnp.asarray(drawn.astype(out[name].dtype))
    for name, factor in factors.items():
        out[name] = (out[name] * factor).astype(out[name].dtype)
    return out
```

```python
from contextlib import ExitStack

import concourse.bass as bass
from concourse import mybir
from concourse.alu_op_type import AluOpType as ALU

P = 128
B = 512
F = 26
D = 128
H1, H2 = 512, 256
BT = B // P
NV = F + 1
VP = 32
STEPS = (F + 3) // 4
QV = 4
QUADS = (NV + QV - 1) // QV
GB = 4
GT = 16
TILES = P // 4 // GT


def dlrm_tower(nc, x, ids, tables, w_pairs, w_dense, w_dense2, w2, b2, w3, y):
    fp32 = mybir.dt.float32
    u32 = mybir.dt.uint32
    ACT = mybir.ActivationFunctionType

    with ExitStack() as ctx:
        def sb(name, shape, dt=fp32):
            return ctx.enter_context(nc.sbuf_tensor(name, shape, dt))

        def pb(name, shape, dt=fp32):
            return ctx.enter_context(nc.psum_tensor(name, shape, dt))

        def sem(name):
            return ctx.enter_context(nc.semaphore(name))

        ids_sb = sb("ids_sb", [P, BT, F], u32)
        x_sb = sb("x_sb", [P, BT, D])
        emb = sb("emb", [P, BT, F, D])
        vecs = sb("vecs", [P, BT, P // 4, 4, VP])
        xt = sb("xt", [P, B])
        gram = sb("gram", [P, STEPS, B])
        wp_sb = sb("wp_sb", [P, STEPS, H1])
        wd_sb = sb("wd_sb", [P, H1])
        wd2_sb = sb("wd2_sb", [P, H1])
        wds_sb = sb("wds_sb", [P, H1])
        w2_sb = sb("w2_sb", [P, H1 // P, H2])
        b2_sb = sb("b2_sb", [P, H2])
        w3_sb = sb("w3_sb", [P, H2])
        h1 = sb("h1", [P, H1])
        h1t = sb("h1t", [P, H1 // P, P])
        h2 = sb("h2", [P, H2])
        h2w = sb("h2w", [P, H2])
        y_sb = sb("y_sb", [P, BT])
        ident = sb("ident", [P, P])

        ps_t = pb("ps_t", [P, 2, QV, P])
        ps_g = pb("ps_g", [P, 4, 512])
        ps_h = pb("ps_h", [P, H1])
        ps_ht = pb("ps_ht", [P, H1 // P, P])

        ids_in = sem("ids_in")
        x_in = sem("x_in")
        wp_in = sem("wp_in")
        wd_in = sem("wd_in")
        w2_in = sem("w2_in")
        tail_in = sem("tail_in")
        emb_in = [[sem(f"emb_in{t}_{q}") for q in range(QUADS)] for t in range(BT)]
        ident_step = sem("ident_step")
        pads_ready = sem("pads_ready")
        wds_ready = sem("wds_ready")
        quad_transposed = sem("quad_transposed")
        quad_kept_act = sem("quad_kept_act")
        quad_kept_dve = sem("quad_kept_dve")
        xt_kept = sem("xt_kept")
        gram_done = sem("gram_done")
        gram_kept_act = sem("gram_kept_act")
        gram_kept_dve = sem("gram_kept_dve")
        h1_done = sem("h1_done")
        h1_kept = sem("h1_kept")
        h1_transposed = sem("h1_transposed")
        h1t_kept = sem("h1t_kept")
        h2_done = sem("h2_done")
        h2_biased = sem("h2_biased")
        y_ready = sem("y_ready")
        y_out = sem("y_out")

        def quad(q):
            return range(q * QV, min(NV, q * QV + QV))

        def acts_quads(n):
            return (n + 1) // 2

        def dves_quads(n):
            return n // 2

        def quad_out(t, q):
            v = quad(q)
            dst = vecs[:, t, :, :, v[0]:v[-1] + 1].rearrange("p g s v -> p v s g")
            src = ps_t[:, (t * QUADS + q) % 2, 0:len(v), :].rearrange("p v (s g) -> p v s g", s=4)
            return dst, src

        def gram_block(t, s, jj):
            bt, half = divmod(t, TILES)
            n = (F - jj + 3) // 4
            src = ps_g[32 * s:32 * s + 32, :, 0:GB * 4 * F].rearrange("p k (g c) -> p k g c", g=GB)
            src = src[:, :, :, s * F + jj:s * F + jj + 4 * (n - 1) + 1:4]
            b0 = bt * P + 32 * s + GT * half
            dst = gram[32 * jj:32 * jj + 32, 0:n, b0:b0 + GT].rearrange("p n (k g) -> p k g n", g=GB)
            return src, dst

        block = ctx.enter_context(nc.Block())

        @block.sync
        def _(sp):
            sp.dma_start(ids_sb[:, :, :], ids.rearrange("(t p) f -> p t f", p=P)).then_inc(ids_in, 16)
            sp.dma_start(x_sb[:, :, :], x.rearrange("(t p) d -> p t d", p=P)).then_inc(x_in, 16)
            sp.dma_start(wd_sb[:, :], w_dense).then_inc(wd_in, 16)
            sp.dma_start(wd2_sb[:, :], w_dense2).then_inc(wd_in, 16)
            sp.dma_start(wp_sb[:, :, :], w_pairs).then_inc(wp_in, 16)
            sp.dma_start(w2_sb[:, :, :], w2.rearrange("(k p) n -> p k n", p=P)).then_inc(w2_in, 16)
            sp.dma_start(b2_sb[:, :], b2.rearrange("(a n) -> a n", a=1).broadcast_to([P, H2])).then_inc(tail_in, 16)
            sp.dma_start(w3_sb[:, :], w3.rearrange("n a -> a n").broadcast_to([P, H2])).then_inc(tail_in, 16)
            for t in range(BT):
                sp.wait_ge(y_ready, t + 1)
                sp.dma_start(y[t * P:(t + 1) * P, :], y_sb[:, t:t + 1]).then_inc(y_out, 16)
            sp.wait_ge(y_out, 16 * BT)

        @block.gpsimd
        def _(pool):
            pool.memset(ident[:, :], 0.0).then_inc(ident_step, 1)
            pool.wait_ge(ident_step, 1)
            pool.affine_select(out=ident[:, :], in_=ident[:, :], compare_op=ALU.not_equal, fill=1.0,
                               base=0, pattern=[[-1, P]], channel_multiplier=1).then_inc(ident_step, 1)
            pool.wait_ge(ids_in, 16)
            for t in range(BT):
                for f in range(F):
                    pool.indirect_dma_start(
                        out=emb[:, t, f, :], out_offset=None, in_=tables[f],
                        in_offset=bass.IndirectOffsetOnAxis(ap=ids_sb[:, t, f:f + 1], axis=0),
                    ).then_inc(emb_in[t][(f + 1) // QV], 16)

        @block.tensor
        def _(pe):
            pe.wait_ge(ident_step, 2)
            pe.wait_ge(x_in, 16)
            for t in range(BT):
                for q in range(QUADS):
                    n = t * QUADS + q
                    pe.wait_ge(emb_in[t][q], 16 * sum(v > 0 for v in quad(q)))
                    if n >= 2:
                        pe.wait_ge(*((quad_kept_act, acts_quads(n - 1)) if n % 2 == 0 else
                                     (quad_kept_dve, dves_quads(n - 1))))
                    for i, v in enumerate(quad(q)):
                        src = x_sb[:, t, :] if v == 0 else emb[:, t, v - 1, :]
                        last = nc.tensor.transpose(ps_t[:, n % 2, i, :], src, ident[:, :])
                    last.then_inc(quad_transposed, 1)
                pe.wait_ge(quad_kept_act, acts_quads((t + 1) * QUADS))
                pe.wait_ge(quad_kept_dve, dves_quads((t + 1) * QUADS))
                pe.wait_ge(pads_ready, 1)
                for half in range(TILES):
                    n = t * TILES + half
                    if n >= 1:
                        pe.wait_ge(gram_kept_act, 8 * n)
                        pe.wait_ge(gram_kept_dve, 8 * n)
                    for k in range(4):
                        for g in range(GB):
                            group = vecs[:, t, GT * half + GB * k + g, :, :]
                            last = nc.tensor.matmul(
                                ps_g[:, k, g * 4 * F:(g + 1) * 4 * F],
                                group.rearrange("p s v -> p (s v)"), group[:, :, 1:NV],
                                start=True, stop=True)
                    last.then_inc(gram_done, 1)
                pe.wait_ge(gram_kept_act, 8 * TILES * (t + 1))
                pe.wait_ge(gram_kept_dve, 8 * TILES * (t + 1))
                pe.wait_ge(xt_kept, t + 1)
                pe.wait_ge(wds_ready, 1)
                pe.wait_ge(wp_in, 16)
                if t:
                    pe.wait_ge(h2_biased, t)
                nc.tensor.matmul(ps_h[:, :], xt[:, t * P:(t + 1) * P], wds_sb[:, :], start=True, stop=False)
                for k in range(STEPS):
                    rows = P if k < STEPS - 1 else 65
                    last = nc.tensor.matmul(ps_h[:, :], gram[0:rows, k, t * P:(t + 1) * P],
                                            wp_sb[0:rows, k, :], start=False, stop=(k == STEPS - 1))
                last.then_inc(h1_done, 1)
                pe.wait_ge(h1_kept, t + 1)
                if t:
                    pe.wait_ge(h1t_kept, t)
                for k in range(H1 // P):
                    last = nc.tensor.transpose(ps_ht[:, k, :], h1[:, k * P:(k + 1) * P], ident[:, :])
                last.then_inc(h1_transposed, 1)
                pe.wait_ge(h1t_kept, t + 1)
                pe.wait_ge(w2_in, 16)
                for k in range(H1 // P):
                    last = nc.tensor.matmul(ps_h[:, 0:H2], h1t[:, k, :], w2_sb[:, k, :],
                                            start=(k == 0), stop=(k == H1 // P - 1))
                last.then_inc(h2_done, 1)

        @block.scalar
        def _(act):
            for t in range(BT):
                for q in range(QUADS):
                    n = t * QUADS + q
                    if n % 2 == 0:
                        act.wait_ge(quad_transposed, n + 1)
                        if q == 0:
                            act.activation(xt[:, t * P:(t + 1) * P], ps_t[:, n % 2, 0, :], ACT.Copy).then_inc(xt_kept, 1)
                        act.activation(*quad_out(t, q), ACT.Copy).then_inc(quad_kept_act, 1)
                for half in range(TILES):
                    n = t * TILES + half
                    act.wait_ge(gram_done, n + 1)
                    for s in range(2):
                        for jj in range(4):
                            src, dst = gram_block(n, s, jj)
                            act.activation(dst, src, ACT.Copy).then_inc(gram_kept_act, 1)
                act.wait_ge(h1_done, t + 1)
                if t:
                    act.wait_ge(h1_transposed, t)
                act.activation(h1[:, :], ps_h[:, :], ACT.Relu).then_inc(h1_kept, 1)

        @block.vector
        def _(dve):
            dve.memset(vecs[:, :, :, :, NV:VP].rearrange("p t g s v -> p (t g s) v"), 0.0)
            dve.memset(gram[64:65, STEPS - 1, :], 1.0).then_inc(pads_ready, 1)
            dve.wait_ge(wd_in, 32)
            dve.tensor_tensor(wds_sb[:, :], wd_sb[:, :], wd2_sb[:, :], ALU.add).then_inc(wds_ready, 1)
            dve.wait_ge(tail_in, 32)
            for t in range(BT):
                for q in range(QUADS):
                    n = t * QUADS + q
                    if n % 2 == 1:
                        dve.wait_ge(quad_transposed, n + 1)
                        if q == 0:
                            dve.tensor_copy(xt[:, t * P:(t + 1) * P], ps_t[:, n % 2, 0, :]).then_inc(xt_kept, 1)
                        dve.tensor_copy(*quad_out(t, q)).then_inc(quad_kept_dve, 1)
                for half in range(TILES):
                    n = t * TILES + half
                    dve.wait_ge(gram_done, n + 1)
                    for s in range(2, 4):
                        for jj in range(4):
                            src, dst = gram_block(n, s, jj)
                            dve.tensor_copy(dst, src).then_inc(gram_kept_dve, 1)
                dve.wait_ge(h1_transposed, t + 1)
                if t:
                    dve.wait_ge(h2_done, t)
                dve.tensor_copy(h1t[:, :, :], ps_ht[:, :, :]).then_inc(h1t_kept, 1)
                dve.wait_ge(h2_done, t + 1)
                dve.tensor_tensor(h2[:, :], ps_h[:, 0:H2], b2_sb[:, :], ALU.add).then_inc(h2_biased, 1)
                dve.wait_ge(h2_biased, t + 1)
                dve.scalar_tensor_tensor(h2w[:, :], h2[:, :], 0.0, w3_sb[:, :], ALU.max, ALU.mult,
                                         accum_out=y_sb[:, t:t + 1]).then_inc(y_ready, 1)


def pair_rows():
    import numpy as np
    bias, zero = 607, 608
    rows = np.full((P, STEPS), zero)
    for j in range(F):
        rows[32 * (j % 4), j // 4] = D + j
        for i in range(j):
            rows[32 * (j % 4) + 1 + i, j // 4] = D + F + i * F - i * (i + 1) // 2 + (j - i - 1)
    rows[64, STEPS - 1] = bias
    return rows


def kernel(**inputs):
    import numpy as np
    import concourse.bacc as bacc
    from concourse.bass_utils import run_bass_kernel_spmd

    nc = bacc.Bacc("TRN2", target_bir_lowering=False, num_devices=1)
    w1 = np.asarray(inputs["W_top1"])
    padded = np.concatenate([w1, np.asarray(inputs["b_top1"])[None], np.zeros((1, H1), w1.dtype)])
    data = {"x": inputs["r_dense_features"], "ids": inputs["ids"]}
    data.update({f"tbl_{f}": inputs[f"tbl_{f}"] for f in range(F)})
    data.update(w_pairs=padded[pair_rows()], w_dense=w1[0:D], w_dense2=w1[w1.shape[0] - D:],
                w2=inputs["W_top2"], b2=inputs["b_top2"], w3=inputs["W_top3"])
    arrays, aps = {}, {}
    for name, value in data.items():
        a = np.ascontiguousarray(value)
        arrays[f"in_{name}"] = a.view(np.uint32) if name == "ids" else a
        a = arrays[f"in_{name}"]
        aps[name] = nc.dram_tensor(f"in_{name}", a.shape, mybir.dt.from_np(a.dtype), kind="ExternalInput").ap()
    y = nc.dram_tensor("out_y", (B, 1), mybir.dt.float32, kind="ExternalOutput").ap()
    dlrm_tower(nc, aps["x"], aps["ids"], [aps[f"tbl_{f}"] for f in range(F)], aps["w_pairs"],
               aps["w_dense"], aps["w_dense2"], aps["w2"], aps["b2"], aps["w3"], y)
    r = run_bass_kernel_spmd(nc, [arrays], core_ids=[0])
    return r.results[0]["out_y"]
```

```python
from contextlib import ExitStack

import concourse.bass as bass
from concourse import mybir
from concourse.alu_op_type import AluOpType as ALU

P = 128
B = 512
ROWS = [125000, 12500, 1000, 1250, 12500, 1000, 1000, 12500, 1250, 1000, 1250, 1000, 1000, 1000,
        1250, 12500, 12500, 1000, 1250, 1250, 12500, 12500, 1000, 1000, 12500, 1000]
F = len(ROWS)
D = 128
H1, H2 = 512, 256
BT = B // P
SEL_ROWS = 1000
SEL = [f for f in range(F) if ROWS[f] == SEL_ROWS][:8]
GAT = [f for f in range(F) if f not in SEL]
ORDER = GAT + SEL
NV = F + 1
VP = 32
SK = 8
SP = SEL_ROWS // SK
AK = 1
VK = SK - AK
PB = 3
IB = 4
OH = 4
OA = 2
STEPS = (F + 3) // 4
QV = 4
NT = len(GAT) + 1
QUADS = (NT + QV - 1) // QV
GB = 4
GT = 16
TILES = P // 4 // GT
KH = H1 // P
PART = SK * D
PAIR_PARTS = (STEPS + 1) // 2
DENSE = len(SEL) + PAIR_PARTS
LAYER2 = DENSE + 1
QUAD_AFTER = 1
EARLY = [divmod(i, QUADS) for i in range(len(SEL) - QUAD_AFTER)]
LATE = [q for q in range(QUADS) if (1, q) not in EARLY]
WARM = 14


def dlrm_tower(nc, x, ids, ids_sel, tables, w_pairs, w_dense, w2, b2, w3, y):
    fp32 = mybir.dt.float32
    fp32r = mybir.dt.float32r
    u32 = mybir.dt.uint32
    i32 = mybir.dt.int32
    ACT = mybir.ActivationFunctionType

    with ExitStack() as ctx:
        def sb(name, shape, dt=fp32):
            return ctx.enter_context(nc.sbuf_tensor(name, shape, dt))

        def pb(name, shape, dt=fp32):
            return ctx.enter_context(nc.psum_tensor(name, shape, dt))

        def sem(name):
            return ctx.enter_context(nc.semaphore(name))

        ids_sb = sb("ids_sb", [P, BT, F], u32)
        x_sb = sb("x_sb", [P, BT, D])
        emb = sb("emb", [P, 2, len(GAT), D])
        ids_all = sb("ids_all", [P, IB, B], i32)
        row_int = sb("row_int", [P, SK], i32)
        row_no = sb("row_no", [P, SK])
        row_neg = sb("row_neg", [P, SK])
        part = sb("part", [P, PB, PART])
        table_hi = sb("table_hi", [P, 2, SK, D], fp32r)
        table_lo = sb("table_lo", [P, 2, SK, D], fp32r)
        onehot = sb("onehot", [P, OH, B], fp32r)
        onehot_a = sb("onehot_a", [P, OA, B], fp32r)
        vecs = sb("vecs", [P, BT, P // 4, 4, VP])
        xt = sb("xt", [P, 2, P])
        xt_hi = sb("xt_hi", [P, B], fp32r)
        xt_lo = sb("xt_lo", [P, B], fp32r)
        gram = sb("gram", [P, STEPS, P])
        gram_hi = sb("gram_hi", [P, 2, STEPS, P], fp32r)
        gram_lo = sb("gram_lo", [P, 2, STEPS, P], fp32r)
        wp_hi = sb("wp_hi", [P, STEPS, H1], fp32r)
        wp_lo = sb("wp_lo", [P, STEPS, H1], fp32r)
        wd_hi = sb("wd_hi", [P, H1], fp32r)
        wd_lo = sb("wd_lo", [P, H1], fp32r)
        w2_hi = sb("w2_hi", [P, KH, H2], fp32r)
        w2_lo = sb("w2_lo", [P, KH, H2], fp32r)
        b2_sb = sb("b2_sb", [P, H2])
        w3_sb = sb("w3_sb", [P, H2])
        h1 = sb("h1", [P, H1])
        h1t_hi = sb("h1t_hi", [P, KH, P], fp32r)
        h1t_lo = sb("h1t_lo", [P, KH, P], fp32r)
        h2 = sb("h2", [P, H2])
        y_sb = sb("y_sb", [P, BT])
        ident = sb("ident", [P, P])
        zeros = sb("zeros", [P, B], mybir.dt.bfloat16)

        ps_t = pb("ps_t", [P, 2, QV, P])
        ps_g = pb("ps_g", [P, 4, 512])
        ps_h = pb("ps_h", [P, H1])
        ps_u = pb("ps_u", [P, H1])

        ids_in = sem("ids_in")
        x_in = sem("x_in")
        ids_all_in = [sem(f"ids_all_in{i}") for i in range(IB)]
        part_in = [sem(f"part_in{i}") for i in range(PB)]
        tail_in = sem("tail_in")
        emb_in = [[sem(f"emb_in{t}_{q}") for q in range(QUADS)] for t in range(BT)]
        ident_step = sem("ident_step")
        zeros_ready = sem("zeros_ready")
        row_int_ready = sem("row_int_ready")
        row_no_ready = sem("row_no_ready")
        row_neg_ready = sem("row_neg_ready")
        pads_ready = sem("pads_ready")
        dense_summed = sem("dense_summed")
        hi_ready = sem("hi_ready")
        lo_ready = sem("lo_ready")
        onehot_ready = sem("onehot_ready")
        distance_ready = sem("distance_ready")
        onehot_a_ready = sem("onehot_a_ready")
        onehot_used = sem("onehot_used")
        sel_kept = sem("sel_kept")
        quad_transposed = sem("quad_transposed")
        quad_kept = sem("quad_kept")
        xt_kept = sem("xt_kept")
        xt_hi_ready = sem("xt_hi_ready")
        xt_lo_ready = sem("xt_lo_ready")
        gram_done = sem("gram_done")
        gram_kept_act = sem("gram_kept_act")
        gram_kept_dve = sem("gram_kept_dve")
        gram_hi_ready = sem("gram_hi_ready")
        gram_lo_ready = sem("gram_lo_ready")
        h1_done = sem("h1_done")
        h1_kept = sem("h1_kept")
        h1_transposed = sem("h1_transposed")
        h1t_hi_ready = sem("h1t_hi_ready")
        h1t_lo_ready = sem("h1t_lo_ready")
        h2_done = sem("h2_done")
        h2_biased = sem("h2_biased")
        y_ready = sem("y_ready")
        y_out = sem("y_out")

        def quad(q):
            return range(q * QV, min(NT, q * QV + QV))

        def quad_out(t, q):
            v = quad(q)
            dst = vecs[:, t, :, :, v[0]:v[-1] + 1].rearrange("p g s v -> p v s g")
            src = ps_t[:, (t * QUADS + q) % 2, 0:len(v), :].rearrange("p v (s g) -> p v s g", s=4)
            return dst, src

        def gram_block(half, s, jj):
            n = (F - jj + 3) // 4
            src = ps_g[32 * s:32 * s + 32, :, 0:GB * 4 * F].rearrange("p k (g c) -> p k g c", g=GB)
            src = src[:, :, :, s * F + jj:s * F + jj + 4 * (n - 1) + 1:4]
            b0 = 32 * s + GT * half
            dst = gram[32 * jj:32 * jj + 32, 0:n, b0:b0 + GT].rearrange("p n (k g) -> p k g n", g=GB)
            return src, dst

        def half_tile(a, half):
            return a.rearrange("p k (s h g) -> p k s h g", s=4, h=TILES)[:, :, :, half, :]

        def part_place(n):
            raw = part[:, n % PB, :]
            if n < len(SEL):
                kd = "p (k d) -> p k d"
                return (raw[0:SP, :].rearrange(kd, k=SK), table_hi[0:SP, n % 2, :, :], table_lo[0:SP, n % 2, :, :])
            if n < DENSE:
                k0 = 2 * (n - len(SEL))
                k1 = min(STEPS, k0 + 2)
                return (raw[:, 0:(k1 - k0) * H1].rearrange("p (k n) -> p k n", k=k1 - k0),
                        wp_hi[:, k0:k1, :], wp_lo[:, k0:k1, :])
            if n == DENSE:
                return raw[:, 0:H1], wd_hi[:, :], wd_lo[:, :]
            return raw.rearrange("p (k n) -> p k n", k=KH), w2_hi[:, :, :], w2_lo[:, :, :]

        def dve_onehot_uses(c):
            return c // VK * SK + c % VK + 1

        block = ctx.enter_context(nc.Block())

        @block.sync
        def _(sp):
            def load_ids(n):
                if n >= IB:
                    sp.wait_ge(onehot_ready, (n - IB + 1) * VK)
                    sp.wait_ge(onehot_a_ready, (n - IB + 1) * AK)
                sp.dma_start(ids_all[:, n % IB, :],
                             ids_sel[n:n + 1, :].broadcast_to([P, B])).then_inc(ids_all_in[n % IB], 16)

            def load_part(n):
                if n >= PB:
                    sp.wait_ge(hi_ready, n - PB + 1)
                    sp.wait_ge(lo_ready, n - PB + 1)
                raw = part_place(n)[0]
                if n < len(SEL):
                    src = tables[SEL[n]].rearrange("(p k) d -> p k d", k=SK)
                elif n < DENSE:
                    k0 = 2 * (n - len(SEL))
                    src = w_pairs[:, k0:min(STEPS, k0 + 2), :]
                elif n == DENSE:
                    raw = part[:, n % PB, :].rearrange("p (a n) -> p a n", a=2)
                    src = w_dense.rearrange("a p n -> p a n")
                else:
                    src = w2.rearrange("(k p) n -> p k n", p=P)
                sp.dma_start(raw, src).then_inc(part_in[n % PB], 16)

            sp.dma_start(ids_sb[:, :, :], ids.rearrange("(t p) f -> p t f", p=P)).then_inc(ids_in, 16)
            load_part(0)
            load_ids(0)
            load_ids(1)
            load_part(1)
            sp.dma_start(x_sb[:, :, :], x.rearrange("(t p) d -> p t d", p=P)).then_inc(x_in, 16)
            for n in range(2, len(SEL)):
                load_ids(n)
                load_part(n)
            for n in range(len(SEL), LAYER2 + 1):
                load_part(n)
            sp.dma_start(b2_sb[:, :], b2.rearrange("(a n) -> a n", a=1).broadcast_to([P, H2])).then_inc(tail_in, 16)
            sp.dma_start(w3_sb[:, :], w3.rearrange("n a -> a n").broadcast_to([P, H2])).then_inc(tail_in, 16)
            for t in range(BT):
                sp.wait_ge(y_ready, t + 1)
                sp.dma_start(y[t * P:(t + 1) * P, :], y_sb[:, t:t + 1]).then_inc(y_out, 16)
            sp.wait_ge(y_out, 16 * BT)

        @block.gpsimd
        def _(pool):
            pool.iota(row_int[:, :], pattern=[[1, SK]], base=0, channel_multiplier=SK).then_inc(row_int_ready, 1)
            pool.memset(ident[:, :], 0.0).then_inc(ident_step, 1)
            pool.wait_ge(ident_step, 1)
            pool.affine_select(out=ident[:, :], in_=ident[:, :], compare_op=ALU.not_equal, fill=1.0,
                               base=0, pattern=[[-1, P]], channel_multiplier=1).then_inc(ident_step, 1)
            pool.wait_ge(ids_in, 16)
            for t in range(BT):
                for i, f in enumerate(GAT):
                    q = (i + 1) // QV
                    if t >= 2 and (i == 0 or (i + 1) % QV == 0):
                        pool.wait_ge(quad_transposed, (t - 2) * QUADS + q + 1)
                    pool.indirect_dma_start(
                        out=emb[:, t % 2, i, :], out_offset=None, in_=tables[f],
                        in_offset=bass.IndirectOffsetOnAxis(ap=ids_sb[:, t, f:f + 1], axis=0),
                    ).then_inc(emb_in[t][q], 16)

        @block.tensor
        def _(pe):
            def select(n):
                pe.wait_ge(hi_ready, n + 1)
                pe.wait_ge(lo_ready, n + 1)
                if n >= 4:
                    pe.wait_ge(sel_kept, n - 3)
                for k in range(SK):
                    if k < VK:
                        pe.wait_ge(onehot_ready, n * VK + k + 1)
                        hot = onehot[0:SP, (n * VK + k) % OH, :]
                    else:
                        c = n * AK + k - VK
                        pe.wait_ge(onehot_a_ready, c + 1)
                        hot = onehot_a[0:SP, c % OA, :]
                    nc.tensor.matmul(ps_g[:, n % 4, :], table_hi[0:SP, n % 2, k, :], hot, start=(k == 0), stop=False)
                    nc.tensor.matmul(ps_g[:, n % 4, :], table_lo[0:SP, n % 2, k, :], hot,
                                     start=False, stop=(k == SK - 1)).then_inc(onehot_used, 1)

            def transpose_quad(t, q):
                n = t * QUADS + q
                if n == 0:
                    pe.wait_ge(ident_step, 2)
                    pe.wait_ge(x_in, 16)
                pe.wait_ge(emb_in[t][q], 16 * sum(v > 0 for v in quad(q)))
                if n >= 2:
                    pe.wait_ge(quad_kept, n - 1)
                for i, v in enumerate(quad(q)):
                    src = x_sb[:, t, :] if v == 0 else emb[:, t % 2, v - 1, :]
                    last = nc.tensor.transpose(ps_t[:, n % 2, i, :], src, ident[:, :])
                last.then_inc(quad_transposed, 1)

            def gram_tile(t, half):
                n = t * TILES + half
                pe.wait_ge(quad_kept, (t + 1) * QUADS)
                if n == 0:
                    pe.wait_ge(sel_kept, len(SEL))
                    pe.wait_ge(pads_ready, 1)
                else:
                    pe.wait_ge(gram_kept_act, 8 * n)
                    pe.wait_ge(gram_kept_dve, 8 * n)
                for k in range(4):
                    for g in range(GB):
                        group = vecs[:, t, GT * half + GB * k + g, :, :]
                        last = nc.tensor.matmul(
                            ps_g[:, k, g * 4 * F:(g + 1) * 4 * F],
                            group.rearrange("p s v -> p (s v)"), group[:, :, 1:NV],
                            start=True, stop=True)
                last.then_inc(gram_done, 1)

            def layer1(t):
                if t == 0:
                    pe.wait_ge(hi_ready, DENSE + 1)
                    pe.wait_ge(lo_ready, DENSE + 1)
                else:
                    pe.wait_ge(h1_kept, t)
                pe.wait_ge(xt_hi_ready, t + 1)
                pe.wait_ge(xt_lo_ready, t + 1)
                cols = slice(t * P, (t + 1) * P)
                nc.tensor.matmul(ps_h[:, :], xt_hi[:, cols], wd_hi[:, :], start=True, stop=False)
                nc.tensor.matmul(ps_h[:, :], xt_hi[:, cols], wd_lo[:, :], start=False, stop=False)
                nc.tensor.matmul(ps_h[:, :], xt_lo[:, cols], wd_hi[:, :], start=False, stop=False)
                rows = [slice(0, P)] * (STEPS - 1) + [slice(0, 65)]
                pe.wait_ge(gram_hi_ready, TILES * (t + 1))
                for k, r in enumerate(rows):
                    nc.tensor.matmul(ps_h[:, :], gram_hi[r, t % 2, k, :], wp_hi[r, k, :], start=False, stop=False)
                    nc.tensor.matmul(ps_h[:, :], gram_hi[r, t % 2, k, :], wp_lo[r, k, :], start=False, stop=False)
                pe.wait_ge(gram_lo_ready, TILES * (t + 1))
                for k, r in enumerate(rows):
                    last = nc.tensor.matmul(ps_h[:, :], gram_lo[r, t % 2, k, :], wp_hi[r, k, :],
                                            start=False, stop=(k == STEPS - 1))
                last.then_inc(h1_done, 1)

            def transpose_h1(t):
                pe.wait_ge(h1_kept, t + 1)
                if t:
                    pe.wait_ge(h2_biased, t)
                for k in range(KH):
                    last = nc.tensor.transpose(ps_u[:, k * P:(k + 1) * P], h1[:, k * P:(k + 1) * P], ident[:, :])
                last.then_inc(h1_transposed, 1)

            def layer2(t):
                if t == 0:
                    pe.wait_ge(hi_ready, LAYER2 + 1)
                    pe.wait_ge(lo_ready, LAYER2 + 1)
                pe.wait_ge(h1t_hi_ready, t + 1)
                pe.wait_ge(h1t_lo_ready, t + 1)
                for k in range(KH):
                    nc.tensor.matmul(ps_u[:, 0:H2], h1t_hi[:, k, :], w2_hi[:, k, :], start=(k == 0), stop=False)
                    nc.tensor.matmul(ps_u[:, 0:H2], h1t_hi[:, k, :], w2_lo[:, k, :], start=False, stop=False)
                    last = nc.tensor.matmul(ps_u[:, 0:H2], h1t_lo[:, k, :], w2_hi[:, k, :],
                                            start=False, stop=(k == KH - 1))
                last.then_inc(h2_done, 1)

            pe.wait_ge(zeros_ready, 1)
            for _ in range(WARM):
                nc.tensor.matmul(ps_h[:, :], zeros[:, 0:P], zeros[:, :], start=True, stop=True)
            for n in range(len(SEL)):
                select(n)
                if n >= QUAD_AFTER:
                    transpose_quad(*EARLY[n - QUAD_AFTER])
            gram_tile(0, 0)
            for q in LATE[:-2]:
                transpose_quad(1, q)
            gram_tile(0, 1)
            for q in LATE[-2:]:
                transpose_quad(1, q)
            for t in range(1, BT - 1):
                gram_tile(t, 0)
                transpose_quad(t + 1, 0)
                layer1(t - 1)
                transpose_quad(t + 1, 1)
                transpose_quad(t + 1, 2)
                transpose_h1(t - 1)
                gram_tile(t, 1)
                layer2(t - 1)
                for q in range(3, QUADS):
                    if (t, q) == (BT - 2, QUADS - 1):
                        layer1(t)
                    transpose_quad(t + 1, q)
            transpose_h1(BT - 2)
            gram_tile(BT - 1, 0)
            layer2(BT - 2)
            gram_tile(BT - 1, 1)
            layer1(BT - 1)
            transpose_h1(BT - 1)
            layer2(BT - 1)

        @block.scalar
        def _(act):
            def split_hi(n):
                act.wait_ge(part_in[n % PB], 16 * (n // PB + 1))
                if 2 <= n < len(SEL):
                    act.wait_ge(onehot_used, SK * (n - 1))
                if n == DENSE:
                    act.wait_ge(dense_summed, 1)
                raw, hi, _lo = part_place(n)
                act.activation(hi, raw, ACT.Copy).then_inc(hi_ready, 1)

            def one_hot(n):
                if n == 0:
                    act.wait_ge(row_neg_ready, 1)
                act.wait_ge(ids_all_in[n % IB], 16 * (n // IB + 1))
                for k in range(VK, SK):
                    c = n * AK + k - VK
                    if c >= OA:
                        act.wait_ge(onehot_used, (c - OA) // AK * SK + VK + (c - OA) % AK + 1)
                    hot = onehot_a[0:SP, c % OA, :]
                    act.activation(hot, ids_all[0:SP, n % IB, :], ACT.Abs,
                                   bias=row_neg[0:SP, k:k + 1]).then_inc(distance_ready, 1)
                    act.wait_ge(distance_ready, c + 1)
                    act.activation(hot, hot.bitcast(fp32), ACT.Relu,
                                   bias=1.0, scale=-1.0).then_inc(onehot_a_ready, 1)

            def keep_selected(n):
                act.wait_ge(onehot_used, SK * (n + 1))
                act.activation(vecs[:, :, :, :, 1 + len(GAT) + n].rearrange("p t g s -> p t s g"),
                               ps_g[:, n % 4, :].rearrange("p (t s g) -> p t s g", t=BT, s=4),
                               ACT.Copy).then_inc(sel_kept, 1)

            def keep_quad(t, q):
                act.wait_ge(quad_transposed, t * QUADS + q + 1)
                if q == 0:
                    cols = slice(t * P, (t + 1) * P)
                    if t >= 2:
                        act.wait_ge(xt_lo_ready, t - 1)
                    act.activation(xt[:, t % 2, :], ps_t[:, (t * QUADS) % 2, 0, :], ACT.Copy).then_inc(xt_kept, 1)
                    act.activation(xt_hi[:, cols], ps_t[:, (t * QUADS) % 2, 0, :], ACT.Copy).then_inc(xt_hi_ready, 1)
                act.activation(*quad_out(t, q), ACT.Copy).then_inc(quad_kept, 1)

            def keep_gram(t, half):
                act.wait_ge(gram_done, t * TILES + half + 1)
                if t:
                    act.wait_ge(gram_lo_ready, (t - 1) * TILES + half + 1)
                for s in range(2):
                    for jj in range(4):
                        src, dst = gram_block(half, s, jj)
                        act.activation(dst, src, ACT.Copy).then_inc(gram_kept_act, 1)

            def split_gram_hi(t, half):
                n = t * TILES + half
                act.wait_ge(gram_kept_act, 8 * (n + 1))
                act.wait_ge(gram_kept_dve, 8 * (n + 1))
                if t >= 2:
                    act.wait_ge(h1_done, t - 1)
                act.activation(half_tile(gram_hi[:, t % 2, :, :], half), half_tile(gram[:, :, :], half),
                               ACT.Copy).then_inc(gram_hi_ready, 1)

            def keep_h1(t):
                act.wait_ge(h1_done, t + 1)
                if t:
                    act.wait_ge(h1_transposed, t)
                act.activation(h1[:, :], ps_h[:, :], ACT.Relu).then_inc(h1_kept, 1)

            def keep_h1t(t):
                act.wait_ge(h1_transposed, t + 1)
                if t:
                    act.wait_ge(h2_done, t)
                act.activation(h1t_hi[:, :, :].rearrange("p k b -> p (k b)"), ps_u[:, :],
                               ACT.Copy).then_inc(h1t_hi_ready, 1)

            split_hi(0)
            split_hi(1)
            one_hot(0)
            for n in range(len(SEL)):
                if n + 1 < len(SEL):
                    one_hot(n + 1)
                keep_selected(n)
                split_hi(n + 2)
                if n >= QUAD_AFTER:
                    keep_quad(*EARLY[n - QUAD_AFTER])
            keep_gram(0, 0)
            split_gram_hi(0, 0)
            split_hi(len(SEL) + 2)
            for q in LATE[:-2]:
                keep_quad(1, q)
            keep_gram(0, 1)
            split_gram_hi(0, 1)
            for q in LATE[-2:]:
                keep_quad(1, q)
            split_hi(len(SEL) + 3)
            split_hi(DENSE)
            for t in range(1, BT - 1):
                keep_gram(t, 0)
                split_gram_hi(t, 0)
                keep_quad(t + 1, 0)
                if t == 1:
                    split_hi(LAYER2)
                keep_h1(t - 1)
                keep_quad(t + 1, 1)
                keep_quad(t + 1, 2)
                keep_h1t(t - 1)
                keep_gram(t, 1)
                split_gram_hi(t, 1)
                for q in range(3, QUADS):
                    if (t, q) == (BT - 2, QUADS - 1):
                        keep_h1(t)
                    keep_quad(t + 1, q)
            keep_h1t(BT - 2)
            keep_gram(BT - 1, 0)
            split_gram_hi(BT - 1, 0)
            keep_gram(BT - 1, 1)
            split_gram_hi(BT - 1, 1)
            keep_h1(BT - 1)
            keep_h1t(BT - 1)

        @block.vector
        def _(dve):
            def split_lo(n):
                if n == DENSE:
                    dve.wait_ge(part_in[n % PB], 16 * (n // PB + 1))
                    both = part[:, n % PB, :].rearrange("p (a n) -> p a n", a=2)
                    dve.tensor_tensor(both[:, 0, :], both[:, 0, :], both[:, 1, :], ALU.add).then_inc(dense_summed, 1)
                dve.wait_ge(hi_ready, n + 1)
                if 2 <= n < len(SEL):
                    dve.wait_ge(onehot_used, SK * (n - 1))
                raw, hi, lo = part_place(n)
                dve.tensor_tensor(lo, raw, hi.bitcast(fp32), ALU.subtract).then_inc(lo_ready, 1)

            def one_hots(n):
                dve.wait_ge(ids_all_in[n % IB], 16 * (n // IB + 1))
                for k in range(VK):
                    c = n * VK + k
                    if c >= OH:
                        dve.wait_ge(onehot_used, dve_onehot_uses(c - OH))
                    dve.tensor_scalar(onehot[0:SP, c % OH, :], ids_all[0:SP, n % IB, :], row_no[0:SP, k:k + 1], None,
                                      ALU.is_equal).then_inc(onehot_ready, 1)

            def keep_gram(t, half):
                dve.wait_ge(gram_done, t * TILES + half + 1)
                if t:
                    dve.wait_ge(gram_hi_ready, (t - 1) * TILES + half + 1)
                    dve.wait_ge(gram_lo_ready, (t - 1) * TILES + half + 1)
                for s in range(2, 4):
                    for jj in range(4):
                        src, dst = gram_block(half, s, jj)
                        dve.tensor_copy(dst, src).then_inc(gram_kept_dve, 1)

            def split_gram_lo(t, half):
                dve.wait_ge(gram_hi_ready, t * TILES + half + 1)
                if t >= 2:
                    dve.wait_ge(h1_done, t - 1)
                dve.tensor_tensor(half_tile(gram_lo[:, t % 2, :, :], half), half_tile(gram[:, :, :], half),
                                  half_tile(gram_hi[:, t % 2, :, :], half).bitcast(fp32),
                                  ALU.subtract).then_inc(gram_lo_ready, 1)

            def split_xt(t):
                cols = slice(t * P, (t + 1) * P)
                dve.wait_ge(xt_kept, t + 1)
                dve.wait_ge(xt_hi_ready, t + 1)
                dve.tensor_tensor(xt_lo[:, cols], xt[:, t % 2, :], xt_hi[:, cols].bitcast(fp32),
                                  ALU.subtract).then_inc(xt_lo_ready, 1)

            def split_h1t(t):
                dve.wait_ge(h1t_hi_ready, t + 1)
                if t:
                    dve.wait_ge(h2_done, t)
                flat = "p k b -> p (k b)"
                dve.tensor_tensor(h1t_lo[:, :, :].rearrange(flat), ps_u[:, :],
                                  h1t_hi[:, :, :].rearrange(flat).bitcast(fp32), ALU.subtract).then_inc(h1t_lo_ready, 1)

            def output(t):
                dve.wait_ge(h2_done, t + 1)
                if t == 0:
                    dve.wait_ge(tail_in, 32)
                dve.tensor_tensor(h2[:, :], ps_u[:, 0:H2], b2_sb[:, :], ALU.add).then_inc(h2_biased, 1)
                dve.wait_ge(h2_biased, t + 1)
                dve.scalar_tensor_tensor(h2[:, :], h2[:, :], 0.0, w3_sb[:, :], ALU.max, ALU.mult,
                                         accum_out=y_sb[:, t:t + 1]).then_inc(y_ready, 1)

            dve.memset(zeros[:, :], 0.0).then_inc(zeros_ready, 1)
            dve.wait_ge(row_int_ready, 1)
            dve.tensor_copy(row_no[:, :], row_int[:, :]).then_inc(row_no_ready, 1)
            dve.tensor_scalar(row_neg[:, :], row_int[:, :], -1.0, None, ALU.mult).then_inc(row_neg_ready, 1)
            dve.memset(gram[64:P, STEPS - 1, :], 1.0)
            dve.memset(vecs[:, :, :, :, NV:VP].rearrange("p t g s v -> p (t g s) v"), 0.0).then_inc(pads_ready, 1)
            dve.wait_ge(row_no_ready, 1)
            split_lo(0)
            for n in range(len(SEL)):
                one_hots(n)
                split_lo(n + 1)
            split_xt(0)
            split_lo(len(SEL) + 1)
            keep_gram(0, 0)
            split_gram_lo(0, 0)
            split_lo(len(SEL) + 2)
            keep_gram(0, 1)
            split_gram_lo(0, 1)
            split_xt(1)
            split_lo(len(SEL) + 3)
            split_lo(DENSE)
            for t in range(1, BT - 1):
                keep_gram(t, 0)
                split_gram_lo(t, 0)
                split_xt(t + 1)
                if t == 1:
                    split_lo(LAYER2)
                split_h1t(t - 1)
                keep_gram(t, 1)
                split_gram_lo(t, 1)
                output(t - 1)
            split_h1t(BT - 2)
            keep_gram(BT - 1, 0)
            split_gram_lo(BT - 1, 0)
            output(BT - 2)
            keep_gram(BT - 1, 1)
            split_gram_lo(BT - 1, 1)
            split_h1t(BT - 1)
            output(BT - 1)


def pair_rows():
    import numpy as np
    bias, zero = 607, 608
    rows = np.full((P, STEPS), zero)
    for j in range(F):
        rows[32 * (j % 4), j // 4] = D + ORDER[j]
        for i in range(j):
            a, b = sorted((ORDER[i], ORDER[j]))
            rows[32 * (j % 4) + 1 + i, j // 4] = D + F + a * F - a * (a + 1) // 2 + (b - a - 1)
    rows[64, STEPS - 1] = bias
    return rows


def kernel(**inputs):
    import numpy as np
    import concourse.bacc as bacc
    from concourse.bass_utils import run_bass_kernel_spmd

    nc = bacc.Bacc("TRN2", target_bir_lowering=False, num_devices=1)
    w1 = np.asarray(inputs["W_top1"])
    padded = np.concatenate([w1, np.asarray(inputs["b_top1"])[None], np.zeros((1, H1), w1.dtype)])
    data = {"x": inputs["r_dense_features"], "ids": inputs["ids"],
            "ids_sel": np.asarray(inputs["ids"])[:, SEL].T}
    data.update({f"tbl_{f}": inputs[f"tbl_{f}"] for f in range(F)})
    data.update(w_pairs=padded[pair_rows()], w_dense=np.stack([w1[:D], w1[-D:]]),
                w2=inputs["W_top2"], b2=inputs["b_top2"], w3=inputs["W_top3"])
    arrays, aps = {}, {}
    for name, value in data.items():
        a = np.ascontiguousarray(value)
        arrays[f"in_{name}"] = a.view(np.uint32) if name == "ids" else a
        a = arrays[f"in_{name}"]
        aps[name] = nc.dram_tensor(f"in_{name}", a.shape, mybir.dt.from_np(a.dtype), kind="ExternalInput").ap()
    y = nc.dram_tensor("out_y", (B, 1), mybir.dt.float32, kind="ExternalOutput").ap()
    dlrm_tower(nc, aps["x"], aps["ids"], aps["ids_sel"], [aps[f"tbl_{f}"] for f in range(F)], aps["w_pairs"],
               aps["w_dense"], aps["w2"], aps["b2"], aps["w3"], y)
    r = run_bass_kernel_spmd(nc, [arrays], core_ids=[0])
    return r.results[0]["out_y"]
```

```python
from contextlib import ExitStack

import concourse.bass as bass
from concourse import mybir
from concourse.alu_op_type import AluOpType as ALU

P = 128
B = 512
ROWS = [125000, 12500, 1000, 1250, 12500, 1000, 1000, 12500, 1250, 1000, 1250, 1000, 1000, 1000,
        1250, 12500, 12500, 1000, 1250, 1250, 12500, 12500, 1000, 1000, 12500, 1000]
F = len(ROWS)
D = 128
H1, H2 = 512, 256
BT = B // P
SEL_ROWS = 1000
SEL = [f for f in range(F) if ROWS[f] == SEL_ROWS][:8]
GAT = [f for f in range(F) if f not in SEL]
VP = 32
SK = 8
SP = SEL_ROWS // SK
AK = 1
VK = SK - AK
PB = 5
IB = 4
OH = 6
OA = 2
STEPS = 5
QV = 4
NT = len(GAT)
QUADS = (NT + QV - 1) // QV
GB = 4

PARTNER0, PARTNERS, APART = 5, 26, 5
COPIES = list(range(11, VP, APART))
GRAM_BLOCKS = [(1, VP, 7, STEPS), (0, VP, 5, STEPS), (2, VP, 8, STEPS), (3, VP - 1, 9, STEPS),
               (1, 6, 6, STEPS), (0, 7, 30, 1)]
BIAS = P - 1
QUAD_AT = [12, 17, 22, 27, PARTNER0]
DENSE_AT = PARTNER0 + NT - 16
SEL_AT = COPIES + list(range(DENSE_AT + 1, 11))
BANK_H, BANK_U, BANK_T = 4, 5, 6
UNITS = [(0, 0, 0, 4), (0, 16, BANK_H, 2), (0, 24, 0, 2)]
UNITS += [(1, 0, 2, 2), (1, 8, 0, 2), (1, 16, 0, 4)]
UNITS += [(2, 0, 0, 2), (2, 8, 2, 2), (2, 16, 0, 2), (2, 24, 2, 2)]
UNITS += [(BT - 1, 0, 0, 2), (BT - 1, 8, 2, 2), (BT - 1, 16, BANK_T, 2), (BT - 1, 24, 0, 2)]
UNITS_OF = [[u for u, unit in enumerate(UNITS) if unit[0] == t] for t in range(BT)]
KH = H1 // P
PART = SK * D
PAIR_PARTS = (STEPS + 1) // 2
DENSE = len(SEL) + PAIR_PARTS
LAYER2 = DENSE + 1
QUAD_AFTER = 1
EARLY = [divmod(i, QUADS) for i in range(len(SEL) - QUAD_AFTER)]
LATE = [q for q in range(QUADS) if (1, q) not in EARLY]
WARM = 10


def dlrm_tower(nc, x, ids, ids_sel, tables, w_pairs, w_dense, w2, b2, w3, y):
    fp32 = mybir.dt.float32
    fp32r = mybir.dt.float32r
    u32 = mybir.dt.uint32
    i32 = mybir.dt.int32
    ACT = mybir.ActivationFunctionType

    with ExitStack() as ctx:
        def sb(name, shape, dt=fp32):
            return ctx.enter_context(nc.sbuf_tensor(name, shape, dt))

        def pb(name, shape, dt=fp32):
            return ctx.enter_context(nc.psum_tensor(name, shape, dt))

        def sem(name):
            return ctx.enter_context(nc.semaphore(name))

        ids_sb = sb("ids_sb", [P, BT, F], u32)
        x_sb = sb("x_sb", [P, B])
        emb = sb("emb", [P, 2, len(GAT), D])
        ids_all = sb("ids_all", [P, IB, B], i32)
        row_int = sb("row_int", [P, SK], i32)
        row_no = sb("row_no", [P, SK])
        row_neg = sb("row_neg", [P, SK])
        part = sb("part", [P, PB, PART])
        table_hi = sb("table_hi", [P, 2, SK, D], fp32r)
        table_lo = sb("table_lo", [P, 2, SK, D], fp32r)
        onehot = sb("onehot", [P, OH, B], fp32r)
        onehot_a = sb("onehot_a", [P, OA, B], fp32r)
        vecs = sb("vecs", [P, BT, P // 4, 4, VP])
        x_hi = sb("x_hi", [P, B], fp32r)
        x_lo = sb("x_lo", [P, B], fp32r)
        gram = sb("gram", [P, STEPS, P])
        gram_hi = sb("gram_hi", [P, 2, STEPS, P], fp32r)
        gram_lo = sb("gram_lo", [P, 2, STEPS, P], fp32r)
        wp_hi = sb("wp_hi", [P, STEPS, H1], fp32r)
        wp_lo = sb("wp_lo", [P, STEPS, H1], fp32r)
        wd_hi = sb("wd_hi", [P, H1], fp32r)
        wd_lo = sb("wd_lo", [P, H1], fp32r)
        w2_hi = sb("w2_hi", [P, KH, H2], fp32r)
        w2_lo = sb("w2_lo", [P, KH, H2], fp32r)
        b2_sb = sb("b2_sb", [P, H2])
        w3_sb = sb("w3_sb", [P, H2])
        h1 = sb("h1", [P, H1])
        h1t_hi = sb("h1t_hi", [P, KH, P], fp32r)
        h1t_lo = sb("h1t_lo", [P, KH, P], fp32r)
        h1t_last = sb("h1t_last", [P, 2, P])
        h2 = sb("h2", [P, H2])
        one = sb("one", [1, P])
        y_sb = sb("y_sb", [P, BT])
        ident = sb("ident", [P, P])
        zeros = sb("zeros", [P, B], mybir.dt.bfloat16)

        ps = pb("ps", [P, 8, 512])
        ps_g = ps[:, 0:4, :]
        ps_h = ps[:, BANK_H, :]
        ps_u = ps[:, BANK_U, :]
        ps_t = ps[:, BANK_T:BANK_T + 2, :].rearrange("p a (v d) -> p a v d", v=QV)

        ps_half = ps[:, 2, 0:H2]
        ps_last = ps[:, 3, 0:H2]

        first_ids_in = sem("first_ids_in")
        ids_in = sem("ids_in")
        x_in = sem("x_in")
        ids_all_in = [sem(f"ids_all_in{i}") for i in range(IB)]
        part_in = [sem(f"part_in{i}") for i in range(PB)]
        tail_in = sem("tail_in")
        emb_in = [[sem(f"emb_in{t}_{q}") for q in range(QUADS)] for t in range(BT)]
        ident_step = sem("ident_step")
        zeros_ready = sem("zeros_ready")
        row_int_ready = sem("row_int_ready")
        row_no_ready = sem("row_no_ready")
        row_neg_ready = sem("row_neg_ready")
        ones_ready = sem("ones_ready")
        one_ready = sem("one_ready")
        h1t_kept_act = sem("h1t_kept_act")
        h1t_kept_dve = sem("h1t_kept_dve")
        repeated = sem("repeated")
        dense_summed = sem("dense_summed")
        first_in = sem("first_in")
        first_hi_ready = sem("first_hi_ready")
        first_lo_ready = sem("first_lo_ready")
        hi_ready = sem("hi_ready")
        lo_ready = sem("lo_ready")
        onehot_ready = sem("onehot_ready")
        distance_ready = sem("distance_ready")
        onehot_a_ready = sem("onehot_a_ready")
        onehot_used = sem("onehot_used")
        sel_kept = sem("sel_kept")
        quad_transposed = sem("quad_transposed")
        quad_kept = sem("quad_kept")
        dense_kept = sem("dense_kept")
        x_hi_ready = sem("x_hi_ready")
        x_lo_ready = sem("x_lo_ready")
        gram_done = sem("gram_done")
        gram_kept_act = sem("gram_kept_act")
        gram_kept_dve = sem("gram_kept_dve")
        gram_hi_ready = sem("gram_hi_ready")
        gram_lo_ready = sem("gram_lo_ready")
        h1_done = sem("h1_done")
        h1_kept = sem("h1_kept")
        h1_transposed = sem("h1_transposed")
        h1t_hi_ready = sem("h1t_hi_ready")
        h1t_lo_ready = sem("h1t_lo_ready")
        h2_done = sem("h2_done")
        h2_biased = sem("h2_biased")
        y_ready = sem("y_ready")
        y_out = sem("y_out")

        def quad(q):
            return range(q * QV, min(NT, q * QV + QV))

        def quad_out(t, q):
            v = quad(q)
            dst = vecs[:, t, :, :, QUAD_AT[q]:QUAD_AT[q] + len(v)].rearrange("p g s v -> p v s g")
            src = ps_t[:, (t * QUADS + q) % 2, 0:len(v), :].rearrange("p v (s g) -> p v s g", s=4)
            return dst, src

        def gram_block(u, s, b):
            _t, g0, bank, banks = UNITS[u]
            quadrant, places, partner, n = GRAM_BLOCKS[b]
            src = ps[VP * s:VP * s + places, bank:bank + banks, 0:GB * 4 * PARTNERS].rearrange(
                "p k (g c) -> p k g c", g=GB)
            c0 = s * PARTNERS + partner - PARTNER0
            src = src[:, :, :, c0:c0 + APART * (n - 1) + 1:APART]
            b0 = VP * s + g0
            dst = gram[VP * quadrant:VP * quadrant + places, 0:n, b0:b0 + GB * banks].rearrange(
                "p n (k g) -> p k g n", g=GB)
            return src, dst

        def gram_copies(u, s, b):
            return (2 * u + s % 2) * len(GRAM_BLOCKS) + b + 1

        def units_before(u):
            t, g0, bank, banks = UNITS[u]
            in_banks = [v + 1 for v in range(u) if UNITS[v][2] < bank + banks and bank < UNITS[v][2] + UNITS[v][3]]
            of_samples = [v + 1 for v in range(u) if UNITS[v][0] == t - 1 and UNITS[v][1] < g0 + GB * banks
                          and g0 < UNITS[v][1] + GB * UNITS[v][3]]
            return max(in_banks, default=0), max(of_samples, default=0)

        def blocks_over(b):
            return [c for c in range(b) if GRAM_BLOCKS[c][0] == GRAM_BLOCKS[b][0]]

        def unit_samples(a, u):
            _t, g0, _bank, banks = UNITS[u]
            return a.rearrange("p k (s g) -> p k s g", s=4)[:, :, :, g0:g0 + GB * banks]

        def part_place(n):
            raw = part[:, n % PB, :]
            if n < len(SEL):
                kd = "p (k d) -> p k d"
                return (raw[0:SP, :].rearrange(kd, k=SK), table_hi[0:SP, n % 2, :, :], table_lo[0:SP, n % 2, :, :])
            if n < DENSE:
                k0 = 2 * (n - len(SEL))
                k1 = min(STEPS, k0 + 2)
                return (raw[:, 0:(k1 - k0) * H1].rearrange("p (k n) -> p k n", k=k1 - k0),
                        wp_hi[:, k0:k1, :], wp_lo[:, k0:k1, :])
            if n == DENSE:
                return raw[:, 0:H1], wd_hi[:, :], wd_lo[:, :]
            return raw.rearrange("p (k n) -> p k n", k=KH), w2_hi[:, :, :], w2_lo[:, :, :]

        def dve_onehot_uses(c):
            return c // VK * SK + c % VK + 1

        block = ctx.enter_context(nc.Block())

        @block.sync
        def _(sp):
            def load_ids(n):
                if n >= IB:
                    sp.wait_ge(onehot_ready, (n - IB + 1) * VK)
                    sp.wait_ge(onehot_a_ready, (n - IB + 1) * AK)
                sp.dma_start(ids_all[:, n % IB, :],
                             ids_sel[n:n + 1, :].broadcast_to([P, B])).then_inc(ids_all_in[n % IB], 16)

            def load_part(n):
                if n >= PB:
                    sp.wait_ge(hi_ready, n - PB + 1)
                    sp.wait_ge(lo_ready, n - PB + 1)
                raw = part_place(n)[0]
                if n < len(SEL):
                    src = tables[SEL[n]].rearrange("(p k) d -> p k d", k=SK)
                elif n < DENSE:
                    k0 = 2 * (n - len(SEL))
                    src = w_pairs[:, k0:min(STEPS, k0 + 2), :]
                elif n == DENSE:
                    raw = part[:, n % PB, :].rearrange("p (a n) -> p a n", a=2)
                    src = w_dense.rearrange("a p n -> p a n")
                else:
                    src = w2.rearrange("(k p) n -> p k n", p=P)
                if n == 0:
                    sp.dma_start(raw[:, 0:SK // 2, :], src[:, 0:SK // 2, :]).then_inc(first_in, 16)
                    raw, src = raw[:, SK // 2:SK, :], src[:, SK // 2:SK, :]
                sp.dma_start(raw, src).then_inc(part_in[n % PB], 16)

            def load_gather_ids(t0, t1, loaded):
                sp.dma_start(ids_sb[:, t0:t1, :],
                             ids[t0 * P:t1 * P, :].rearrange("(t p) f -> p t f", p=P)).then_inc(loaded, 16)

            load_gather_ids(0, 1, first_ids_in)
            load_ids(0)
            load_part(0)
            load_part(1)
            load_ids(1)
            load_gather_ids(1, BT, ids_in)
            sp.dma_start(x_sb[:, :], x).then_inc(x_in, 16)
            for n in range(2, len(SEL)):
                load_ids(n)
                load_part(n)
            for n in range(len(SEL), LAYER2 + 1):
                load_part(n)
            sp.dma_start(b2_sb[:, :], b2.rearrange("(a n) -> a n", a=1).broadcast_to([P, H2])).then_inc(tail_in, 16)
            sp.dma_start(w3_sb[:, :], w3.rearrange("n a -> a n").broadcast_to([P, H2])).then_inc(tail_in, 16)
            for t in range(BT):
                sp.wait_ge(y_ready, t + 1)
                sp.dma_start(y[t * P:(t + 1) * P, :], y_sb[:, t:t + 1]).then_inc(y_out, 16)
            sp.wait_ge(y_out, 16 * BT)

        @block.gpsimd
        def _(pool):
            pool.iota(row_int[:, :], pattern=[[1, SK]], base=0, channel_multiplier=SK).then_inc(row_int_ready, 1)
            pool.memset(ident[:, :], 0.0).then_inc(ident_step, 1)
            pool.wait_ge(ident_step, 1)
            pool.affine_select(out=ident[:, :], in_=ident[:, :], compare_op=ALU.not_equal, fill=1.0,
                               base=0, pattern=[[-1, P]], channel_multiplier=1).then_inc(ident_step, 1)
            for t in range(BT):
                pool.wait_ge(ids_in if t else first_ids_in, 16)
                for i, f in enumerate(GAT):
                    q = i // QV
                    if t >= 2 and i % QV == 0:
                        pool.wait_ge(quad_transposed, (t - 2) * QUADS + q + 1)
                    pool.indirect_dma_start(
                        out=emb[:, t % 2, i, :], out_offset=None, in_=tables[f],
                        in_offset=bass.IndirectOffsetOnAxis(ap=ids_sb[:, t, f:f + 1], axis=0),
                    ).then_inc(emb_in[t][q], 16)

        @block.tensor
        def _(pe):
            def select(n):
                if n:
                    pe.wait_ge(hi_ready, n + 1)
                    pe.wait_ge(lo_ready, n + 1)
                else:
                    pe.wait_ge(first_hi_ready, 1)
                if n >= 4:
                    pe.wait_ge(sel_kept, n - 3)
                for k in range(SK):
                    if k < VK:
                        pe.wait_ge(onehot_ready, n * VK + k + 1)
                        hot = onehot[0:SP, (n * VK + k) % OH, :]
                    else:
                        c = n * AK + k - VK
                        pe.wait_ge(onehot_a_ready, c + 1)
                        hot = onehot_a[0:SP, c % OA, :]
                    if (n, k) == (0, SK // 2):
                        pe.wait_ge(hi_ready, 1)
                    nc.tensor.matmul(ps_g[:, n % 4, :], table_hi[0:SP, n % 2, k, :], hot, start=(k == 0), stop=False)
                    if n == 0 and k % (SK // 2) == 0:
                        pe.wait_ge(*((lo_ready, 1) if k else (first_lo_ready, 1)))
                    nc.tensor.matmul(ps_g[:, n % 4, :], table_lo[0:SP, n % 2, k, :], hot,
                                     start=False, stop=(k == SK - 1)).then_inc(onehot_used, 1)

            def transpose_quad(t, q):
                n = t * QUADS + q
                if n == 0:
                    pe.wait_ge(ident_step, 2)
                pe.wait_ge(emb_in[t][q], 16 * len(quad(q)))
                if n >= 2:
                    pe.wait_ge(quad_kept, n - 1)
                for i, v in enumerate(quad(q)):
                    last = nc.tensor.transpose(ps_t[:, n % 2, i, :], emb[:, t % 2, v, :], ident[:, :])
                last.then_inc(quad_transposed, 1)

            def gram_unit(u):
                t, g0, bank, banks = UNITS[u]
                pe.wait_ge(quad_kept, (t + 1) * QUADS)
                pe.wait_ge(repeated, t + 1)
                if u == 0:
                    pe.wait_ge(dense_kept, 1)
                    pe.wait_ge(sel_kept, len(SEL))
                before = units_before(u)[0]
                if before:
                    pe.wait_ge(gram_kept_act, gram_copies(before, 0, -1))
                    pe.wait_ge(gram_kept_dve, gram_copies(before, 0, -1))
                for k in range(banks):
                    for g in range(GB):
                        group = vecs[:, t, g0 + GB * k + g, :, :]
                        last = nc.tensor.matmul(
                            ps[:, bank + k, g * 4 * PARTNERS:(g + 1) * 4 * PARTNERS],
                            group.rearrange("p s v -> p (s v)"), group[:, :, PARTNER0:PARTNER0 + PARTNERS],
                            start=True, stop=True)
                last.then_inc(gram_done, 1)

            def layer1_dense(t, out, n):
                cols = slice(t * P, (t + 1) * P)
                nc.tensor.matmul(out, x_hi[:, cols], wd_hi[:, n], start=True, stop=False)
                nc.tensor.matmul(out, x_hi[:, cols], wd_lo[:, n], start=False, stop=False)
                nc.tensor.matmul(out, x_lo[:, cols], wd_hi[:, n], start=False, stop=False)

            def layer1_pairs_hi(t, out, n, k0=0, k1=STEPS):
                pe.wait_ge(gram_hi_ready, UNITS_OF[t][-1] + 1)
                for k in range(k0, k1):
                    nc.tensor.matmul(out, gram_hi[:, t % 2, k, :], wp_hi[:, k, n], start=False, stop=False)
                    nc.tensor.matmul(out, gram_hi[:, t % 2, k, :], wp_lo[:, k, n], start=False, stop=False)

            def layer1_pairs_lo(t, out, n):
                pe.wait_ge(gram_lo_ready, UNITS_OF[t][-1] + 1)
                for k in range(STEPS):
                    last = nc.tensor.matmul(out, gram_lo[:, t % 2, k, :], wp_hi[:, k, n],
                                            start=False, stop=(k == STEPS - 1))
                last.then_inc(h1_done, 1)

            def layer1_begin(t):
                if t == 0:
                    pe.wait_ge(hi_ready, DENSE + 1)
                    pe.wait_ge(lo_ready, DENSE + 1)
                    pe.wait_ge(x_hi_ready, 1)
                    pe.wait_ge(x_lo_ready, 1)
                    pe.wait_ge(gram_kept_act, gram_copies(2, 0, -1))
                    pe.wait_ge(gram_kept_dve, gram_copies(2, 0, -1))
                else:
                    pe.wait_ge(h1_kept, t)

            def layer1(t):
                layer1_begin(t)
                layer1_dense(t, ps_h[:, :], slice(0, H1))
                layer1_pairs_hi(t, ps_h[:, :], slice(0, H1))
                layer1_pairs_lo(t, ps_h[:, :], slice(0, H1))

            def transpose_h1(t, k0=0, k1=KH):
                pe.wait_ge(h1_kept, t + 1 + k0 // 2)
                if t:
                    pe.wait_ge(h2_biased, t)
                for k in range(k0, k1):
                    last = nc.tensor.transpose(ps_u[:, k * P:(k + 1) * P], h1[:, k * P:(k + 1) * P], ident[:, :])
                last.then_inc(h1_transposed, 1)

            def layer2(t, out, k0=0, k1=KH):
                if t == 0:
                    pe.wait_ge(hi_ready, LAYER2 + 1)
                    pe.wait_ge(lo_ready, LAYER2 + 1)
                halves = k0 // 2 if t == BT - 1 else 0
                pe.wait_ge(h1t_hi_ready, t + 1 + halves)
                pe.wait_ge(h1t_lo_ready, t + 1 + halves)
                for k in range(k0, k1):
                    nc.tensor.matmul(out, h1t_hi[:, k, :], w2_hi[:, k, :],
                                     start=(k == 0 and t < BT - 1), stop=False)
                    nc.tensor.matmul(out, h1t_hi[:, k, :], w2_lo[:, k, :], start=False, stop=False)
                    last = nc.tensor.matmul(out, h1t_lo[:, k, :], w2_hi[:, k, :], start=False, stop=(k == KH - 1))
                if k1 == KH:
                    last.then_inc(h2_done, 1)

            pe.wait_ge(zeros_ready, 1)
            for _ in range(WARM):
                nc.tensor.matmul(ps_h[:, :], zeros[:, 0:P], zeros[:, :], start=True, stop=True)
            for n in range(len(SEL)):
                select(n)
                if n >= QUAD_AFTER:
                    transpose_quad(*EARLY[n - QUAD_AFTER])
            transpose_quad(1, LATE[0])
            gram_unit(0)
            for q in LATE[1:]:
                transpose_quad(1, q)
            gram_unit(1)
            gram_unit(2)
            gram_unit(UNITS_OF[1][0])
            transpose_quad(2, 0)
            gram_unit(UNITS_OF[1][1])
            layer1(0)
            transpose_quad(2, 1)
            transpose_h1(0)
            gram_unit(UNITS_OF[1][2])
            transpose_quad(2, 2)
            transpose_quad(2, 3)
            layer2(0, ps_u[:, 0:H2])
            layer1_begin(1)
            layer1_dense(1, ps_h[:, :], slice(0, H1))
            transpose_quad(2, 4)
            layer1_pairs_hi(1, ps_h[:, :], slice(0, H1))
            layer1_pairs_lo(1, ps_h[:, :], slice(0, H1))
            gram_unit(UNITS_OF[2][0])
            transpose_h1(1)
            transpose_quad(3, 0)
            gram_unit(UNITS_OF[2][1])
            gram_unit(UNITS_OF[2][2])
            transpose_quad(3, 1)
            gram_unit(UNITS_OF[2][3])
            layer2(1, ps_u[:, 0:H2])
            layer1_begin(2)
            layer1_dense(2, ps_h[:, :], slice(0, H1))
            transpose_quad(3, 2)
            layer1_pairs_hi(2, ps_h[:, :], slice(0, H1))
            transpose_quad(3, 3)
            layer1_pairs_lo(2, ps_h[:, :], slice(0, H1))
            transpose_quad(3, 4)
            transpose_h1(2)
            t = BT - 1
            first, second = (ps_h[:, 0:H2], slice(0, H2)), (ps_half, slice(H2, H1))
            layer1_begin(t)
            layer1_dense(t, *first)
            for u in UNITS_OF[t]:
                gram_unit(u)
            pe.wait_ge(gram_kept_act, gram_copies(UNITS_OF[t][2], 0, -1))
            pe.wait_ge(gram_kept_dve, gram_copies(UNITS_OF[t][2], 0, -1))
            layer1_dense(t, *second)
            layer2(t - 1, ps_u[:, 0:H2])
            pe.wait_ge(one_ready, 1)
            pe.wait_ge(tail_in, 32)
            nc.tensor.matmul(ps_last, one[:, :], b2_sb[0:1, :], start=True, stop=False)
            layer1_pairs_hi(t, *first)
            layer1_pairs_lo(t, *first)
            layer1_pairs_hi(t, *second, 0, 3)
            transpose_h1(t, 0, KH // 2)
            layer1_pairs_hi(t, *second, 3, STEPS)
            layer1_pairs_lo(t, *second)
            layer2(t, ps_last, 0, 1)
            pe.wait_ge(h1_kept, BT + 1)
            nc.tensor.transpose(ps_u[:, 0:P], h1[:, 2 * P:3 * P], ident[:, :]).then_inc(h1_transposed, 1)
            nc.tensor.transpose(ps_h[:, 0:P], h1[:, 3 * P:4 * P], ident[:, :]).then_inc(h1_transposed, 1)
            layer2(t, ps_last, 1, 2)
            pe.wait_ge(h1t_kept_act, 1)
            nc.tensor.matmul(ps_last, h1t_last[:, 0, :], part_place(LAYER2)[0][:, 2, :], start=False, stop=False)
            pe.wait_ge(h1t_kept_dve, 1)
            nc.tensor.matmul(ps_last, h1t_last[:, 1, :], part_place(LAYER2)[0][:, 3, :],
                             start=False, stop=True).then_inc(h2_done, 1)

        @block.scalar
        def _(act):
            def split_hi(n):
                if 2 <= n < len(SEL):
                    act.wait_ge(onehot_used, SK * (n - 1))
                if n == DENSE:
                    act.wait_ge(dense_summed, 1)
                raw, hi, _lo = part_place(n)
                if n == 0:
                    act.wait_ge(first_in, 16)
                    act.activation(hi[:, 0:SK // 2, :], raw[:, 0:SK // 2, :], ACT.Copy).then_inc(first_hi_ready, 1)
                    raw, hi = raw[:, SK // 2:SK, :], hi[:, SK // 2:SK, :]
                act.wait_ge(part_in[n % PB], 16 * (n // PB + 1))
                act.activation(hi, raw, ACT.Copy).then_inc(hi_ready, 1)

            def one_hot(n):
                if n == 0:
                    act.wait_ge(row_neg_ready, 1)
                act.wait_ge(ids_all_in[n % IB], 16 * (n // IB + 1))
                for k in range(VK, SK):
                    c = n * AK + k - VK
                    if c >= OA:
                        act.wait_ge(onehot_used, (c - OA) // AK * SK + VK + (c - OA) % AK + 1)
                    hot = onehot_a[0:SP, c % OA, :]
                    act.activation(hot, ids_all[0:SP, n % IB, :], ACT.Abs,
                                   bias=row_neg[0:SP, k:k + 1]).then_inc(distance_ready, 1)
                    act.wait_ge(distance_ready, c + 1)
                    act.activation(hot, hot.bitcast(fp32), ACT.Relu,
                                   bias=1.0, scale=-1.0).then_inc(onehot_a_ready, 1)

            def keep_vectors(place, src, kept):
                act.activation(vecs[:, :, :, :, place].rearrange("p t g s -> p t s g"),
                               src.rearrange("p (t s g) -> p t s g", t=BT, s=4), ACT.Copy).then_inc(kept, 1)

            def keep_selected(n):
                act.wait_ge(onehot_used, SK * (n + 1))
                keep_vectors(SEL_AT[n], ps_g[:, n % 4, :], sel_kept)

            def keep_dense():
                act.wait_ge(x_in, 16)
                keep_vectors(DENSE_AT, x_sb[:, :], dense_kept)
                act.activation(x_hi[:, :], x_sb[:, :], ACT.Copy).then_inc(x_hi_ready, 1)

            def repeat_vectors(t):
                act.wait_ge(sel_kept, len(COPIES))
                act.activation(vecs[:, t, :, :, 0:len(COPIES)], vecs[:, t, :, :, COPIES[0]:VP:APART],
                               ACT.Copy).then_inc(repeated, 1)

            def keep_quad(t, q):
                act.wait_ge(quad_transposed, t * QUADS + q + 1)
                act.activation(*quad_out(t, q), ACT.Copy).then_inc(quad_kept, 1)

            def keep_gram(u):
                act.wait_ge(gram_done, u + 1)
                if u == 0:
                    act.wait_ge(ones_ready, 1)
                before = units_before(u)[1]
                if before:
                    act.wait_ge(gram_lo_ready, before)
                for s in range(2):
                    for b in range(len(GRAM_BLOCKS)):
                        src, dst = gram_block(u, s, b)
                        for c in blocks_over(b):
                            act.wait_ge(gram_kept_act, gram_copies(u, s, c))
                        act.activation(dst, src, ACT.Copy).then_inc(gram_kept_act, 1)

            def split_gram_hi(u):
                t = UNITS[u][0]
                act.wait_ge(gram_kept_act, gram_copies(u + 1, 0, -1))
                act.wait_ge(gram_kept_dve, gram_copies(u + 1, 0, -1))
                if t >= 2:
                    act.wait_ge(h1_done, t - 1)
                act.activation(unit_samples(gram_hi[:, t % 2, :, :], u), unit_samples(gram[:, :, :], u),
                               ACT.Copy).then_inc(gram_hi_ready, 1)

            def keep_h1(t, src, n=slice(0, H1)):
                act.wait_ge(h1_done, t + 1 + n.start // H2)
                if t:
                    act.wait_ge(h1_transposed, t)
                act.activation(h1[:, n], src, ACT.Relu).then_inc(h1_kept, 1)

            def keep_h1t(t, k0=0, k1=KH):
                act.wait_ge(h1_transposed, t + 1 + k0 // 2)
                if t:
                    act.wait_ge(h2_done, t)
                act.activation(h1t_hi[:, k0:k1, :].rearrange("p k b -> p (k b)"), ps_u[:, k0 * P:k1 * P],
                               ACT.Copy).then_inc(h1t_hi_ready, 1)

            split_hi(0)
            one_hot(0)
            split_hi(1)
            for n in range(len(SEL)):
                if n + 1 < len(SEL):
                    one_hot(n + 1)
                if n == 0:
                    keep_dense()
                keep_selected(n)
                split_hi(n + 2)
                if n >= QUAD_AFTER:
                    keep_quad(*EARLY[n - QUAD_AFTER])
                if n >= len(COPIES):
                    repeat_vectors(n - len(COPIES))
            split_hi(len(SEL) + 2)
            keep_quad(1, LATE[0])
            keep_gram(0)
            for q in LATE[1:]:
                keep_quad(1, q)
            keep_gram(1)
            split_gram_hi(0)
            split_hi(DENSE)
            split_gram_hi(1)
            keep_gram(2)
            split_gram_hi(2)
            for t in range(len(SEL) - len(COPIES), BT):
                repeat_vectors(t)
            keep_gram(UNITS_OF[1][0])
            split_gram_hi(UNITS_OF[1][0])
            keep_quad(2, 0)
            keep_gram(UNITS_OF[1][1])
            split_gram_hi(UNITS_OF[1][1])
            keep_h1(0, ps_h[:, :])
            keep_quad(2, 1)
            keep_h1t(0)
            split_hi(LAYER2)
            keep_gram(UNITS_OF[1][2])
            keep_quad(2, 2)
            keep_quad(2, 3)
            split_gram_hi(UNITS_OF[1][2])
            keep_quad(2, 4)
            keep_h1(1, ps_h[:, :])
            keep_gram(UNITS_OF[2][0])
            keep_h1t(1)
            keep_quad(3, 0)
            keep_gram(UNITS_OF[2][1])
            split_gram_hi(UNITS_OF[2][0])
            split_gram_hi(UNITS_OF[2][1])
            keep_gram(UNITS_OF[2][2])
            keep_quad(3, 1)
            keep_gram(UNITS_OF[2][3])
            split_gram_hi(UNITS_OF[2][2])
            split_gram_hi(UNITS_OF[2][3])
            keep_quad(3, 2)
            keep_quad(3, 3)
            keep_h1(2, ps_h[:, :])
            keep_quad(3, 4)
            keep_h1t(2)
            t = BT - 1
            keep_gram(UNITS_OF[t][0])
            keep_gram(UNITS_OF[t][1])
            split_gram_hi(UNITS_OF[t][0])
            keep_gram(UNITS_OF[t][2])
            split_gram_hi(UNITS_OF[t][1])
            split_gram_hi(UNITS_OF[t][2])
            keep_gram(UNITS_OF[t][3])
            split_gram_hi(UNITS_OF[t][3])
            keep_h1(t, ps_h[:, 0:H2], slice(0, H2))
            keep_h1t(t, 0, KH // 2)
            keep_h1(t, ps_half, slice(H2, H1))
            act.wait_ge(h1_transposed, BT + 1)
            act.activation(h1t_last[:, 0, :], ps_u[:, 0:P], ACT.Copy).then_inc(h1t_kept_act, 1)

        @block.vector
        def _(dve):
            def sum_dense():
                dve.wait_ge(part_in[DENSE % PB], 16 * (DENSE // PB + 1))
                both = part[:, DENSE % PB, :].rearrange("p (a n) -> p a n", a=2)
                dve.tensor_tensor(both[:, 0, :], both[:, 0, :], both[:, 1, :], ALU.add).then_inc(dense_summed, 1)

            def split_lo(n):
                raw, hi, lo = part_place(n)
                dve.wait_ge(hi_ready, n + 1)
                if 2 <= n < len(SEL):
                    dve.wait_ge(onehot_used, SK * (n - 1))
                if n == 0:
                    raw, hi, lo = (a[:, SK // 2:SK, :] for a in (raw, hi, lo))
                dve.tensor_tensor(lo, raw, hi.bitcast(fp32), ALU.subtract).then_inc(lo_ready, 1)

            def split_first_lo():
                dve.wait_ge(first_hi_ready, 1)
                raw, hi, lo = (a[:, 0:SK // 2, :] for a in part_place(0))
                dve.tensor_tensor(lo, raw, hi.bitcast(fp32), ALU.subtract).then_inc(first_lo_ready, 1)

            def one_hots(n):
                dve.wait_ge(ids_all_in[n % IB], 16 * (n // IB + 1))
                for k in range(VK):
                    if (n, k) == (0, 3):
                        split_first_lo()
                    if (n, k) == (0, 5):
                        split_lo(0)
                    c = n * VK + k
                    if c >= OH:
                        dve.wait_ge(onehot_used, dve_onehot_uses(c - OH))
                    dve.tensor_scalar(onehot[0:SP, c % OH, :], ids_all[0:SP, n % IB, :], row_no[0:SP, k:k + 1], None,
                                      ALU.is_equal).then_inc(onehot_ready, 1)

            def keep_gram(u):
                dve.wait_ge(gram_done, u + 1)
                if u == 0:
                    dve.wait_ge(ones_ready, 1)
                before = units_before(u)[1]
                if before:
                    dve.wait_ge(gram_hi_ready, before)
                    dve.wait_ge(gram_lo_ready, before)
                for s in range(2, 4):
                    for b in range(len(GRAM_BLOCKS)):
                        src, dst = gram_block(u, s, b)
                        for c in blocks_over(b):
                            dve.wait_ge(gram_kept_dve, gram_copies(u, s, c))
                        dve.tensor_copy(dst, src).then_inc(gram_kept_dve, 1)

            def split_gram_lo(u):
                t = UNITS[u][0]
                dve.wait_ge(gram_hi_ready, u + 1)
                if t >= 2:
                    dve.wait_ge(h1_done, t - 1)
                dve.tensor_tensor(unit_samples(gram_lo[:, t % 2, :, :], u), unit_samples(gram[:, :, :], u),
                                  unit_samples(gram_hi[:, t % 2, :, :], u).bitcast(fp32),
                                  ALU.subtract).then_inc(gram_lo_ready, 1)

            def split_dense():
                dve.wait_ge(x_hi_ready, 1)
                dve.tensor_tensor(x_lo[:, :], x_sb[:, :], x_hi[:, :].bitcast(fp32), ALU.subtract).then_inc(x_lo_ready, 1)

            def split_h1t(t, k0=0, k1=KH):
                dve.wait_ge(h1t_hi_ready, t + 1 + k0 // 2)
                if t:
                    dve.wait_ge(h2_done, t)
                flat = "p k b -> p (k b)"
                dve.tensor_tensor(h1t_lo[:, k0:k1, :].rearrange(flat), ps_u[:, k0 * P:k1 * P],
                                  h1t_hi[:, k0:k1, :].rearrange(flat).bitcast(fp32),
                                  ALU.subtract).then_inc(h1t_lo_ready, 1)

            def output(t, src):
                dve.wait_ge(h2_done, t + 1)
                if t == 0:
                    dve.wait_ge(tail_in, 32)
                dve.tensor_tensor(h2[:, :], src, b2_sb[:, :], ALU.add).then_inc(h2_biased, 1)
                dve.wait_ge(h2_biased, t + 1)
                weigh(t, h2[:, :])

            def weigh(t, src):
                dve.scalar_tensor_tensor(h2[:, :], src, 0.0, w3_sb[:, :], ALU.max, ALU.mult,
                                         accum_out=y_sb[:, t:t + 1]).then_inc(y_ready, 1)

            dve.memset(zeros[:, :], 0.0).then_inc(zeros_ready, 1)
            dve.memset(one[:, :], 1.0).then_inc(one_ready, 1)
            dve.wait_ge(row_int_ready, 1)
            dve.tensor_copy(row_no[:, :], row_int[:, :]).then_inc(row_no_ready, 1)
            dve.tensor_scalar(row_neg[:, :], row_int[:, :], -1.0, None, ALU.mult).then_inc(row_neg_ready, 1)
            dve.memset(gram[3 * VP:P, :, :], 1.0).then_inc(ones_ready, 1)
            dve.wait_ge(row_no_ready, 1)
            for n in range(len(SEL)):
                one_hots(n)
                split_lo(n + 1)
            split_dense()
            split_lo(len(SEL) + 1)
            split_lo(len(SEL) + 2)
            keep_gram(0)
            sum_dense()
            keep_gram(1)
            split_gram_lo(0)
            keep_gram(2)
            split_lo(DENSE)
            split_gram_lo(1)
            split_gram_lo(2)
            for u in UNITS_OF[1][:2]:
                keep_gram(u)
                split_gram_lo(u)
            split_h1t(0)
            split_lo(LAYER2)
            keep_gram(UNITS_OF[1][2])
            split_gram_lo(UNITS_OF[1][2])
            output(0, ps_u[:, 0:H2])
            keep_gram(UNITS_OF[2][0])
            split_h1t(1)
            keep_gram(UNITS_OF[2][1])
            split_gram_lo(UNITS_OF[2][0])
            keep_gram(UNITS_OF[2][2])
            split_gram_lo(UNITS_OF[2][1])
            keep_gram(UNITS_OF[2][3])
            split_gram_lo(UNITS_OF[2][2])
            split_gram_lo(UNITS_OF[2][3])
            output(1, ps_u[:, 0:H2])
            split_h1t(2)
            t = BT - 1
            keep_gram(UNITS_OF[t][0])
            keep_gram(UNITS_OF[t][1])
            split_gram_lo(UNITS_OF[t][0])
            keep_gram(UNITS_OF[t][2])
            split_gram_lo(UNITS_OF[t][1])
            keep_gram(UNITS_OF[t][3])
            split_gram_lo(UNITS_OF[t][2])
            split_gram_lo(UNITS_OF[t][3])
            output(2, ps_u[:, 0:H2])
            split_h1t(t, 0, KH // 2)
            dve.wait_ge(h1_transposed, BT + 2)
            dve.tensor_copy(h1t_last[:, 1, :], ps_h[:, 0:P]).then_inc(h1t_kept_dve, 1)
            dve.wait_ge(h2_done, BT)
            weigh(t, ps_last)


def pair_rows():
    import numpy as np
    bias, zero = 607, 608
    at = {}
    for q, first in enumerate(QUAD_AT):
        at.update({first + i: 1 + f for i, f in enumerate(GAT[q * QV:(q + 1) * QV])})
    at[DENSE_AT] = 0
    at.update({place: 1 + f for place, f in zip(SEL_AT, SEL)})
    at.update({i: at[place] for i, place in enumerate(COPIES)})
    product = {}
    for quadrant, places, partner, n in GRAM_BLOCKS:
        for k in range(n):
            for place in range(places):
                product[VP * quadrant + place, k] = frozenset((at[place], at[partner + APART * k]))
    rows = np.full((P, STEPS), zero)
    where = {pair: entry for entry, pair in product.items()}
    for b in range(1, F + 1):
        rows[where[frozenset((0, b))]] = D + b - 1
        for a in range(1, b):
            rows[where[frozenset((a, b))]] = D + F + (a - 1) * F - a * (a - 1) // 2 + (b - a - 1)
    rows[BIAS, 0] = bias
    return rows


def kernel(**inputs):
    import numpy as np
    import concourse.bacc as bacc
    from concourse.bass_utils import run_bass_kernel_spmd

    nc = bacc.Bacc("TRN2", target_bir_lowering=False, num_devices=1)
    w1 = np.asarray(inputs["W_top1"])
    padded = np.concatenate([w1, np.asarray(inputs["b_top1"])[None], np.zeros((1, H1), w1.dtype)])
    data = {"x": np.asarray(inputs["r_dense_features"]).T, "ids": inputs["ids"],
            "ids_sel": np.asarray(inputs["ids"])[:, SEL].T}
    data.update({f"tbl_{f}": inputs[f"tbl_{f}"] for f in range(F)})
    data.update(w_pairs=padded[pair_rows()], w_dense=np.stack([w1[:D], w1[-D:]]),
                w2=inputs["W_top2"], b2=inputs["b_top2"], w3=inputs["W_top3"])
    arrays, aps = {}, {}
    for name, value in data.items():
        a = np.ascontiguousarray(value)
        arrays[f"in_{name}"] = a.view(np.uint32) if name == "ids" else a
        a = arrays[f"in_{name}"]
        aps[name] = nc.dram_tensor(f"in_{name}", a.shape, mybir.dt.from_np(a.dtype), kind="ExternalInput").ap()
    y = nc.dram_tensor("out_y", (B, 1), mybir.dt.float32, kind="ExternalOutput").ap()
    dlrm_tower(nc, aps["x"], aps["ids"], aps["ids_sel"], [aps[f"tbl_{f}"] for f in range(F)], aps["w_pairs"],
               aps["w_dense"], aps["w2"], aps["b2"], aps["w3"], y)
    r = run_bass_kernel_spmd(nc, [arrays], core_ids=[0])
    return r.results[0]["out_y"]
```
